# Optimizing a Trainium2 kernel written in Bass

```python
import numpy as np
import jax
import jax.numpy as jnp

def _softmax(x, axis=-1):
    return jax.nn.softmax(x, axis=axis)

def _gelu(x):
    return jax.nn.gelu(x, approximate=True)

def _silu(x):
    return jax.nn.silu(x)

def _sigmoid(x):
    return jax.nn.sigmoid(x)

def _layernorm(x, axis=-1, eps=1e-05):
    m = jnp.mean(x, axis=axis, keepdims=True)
    v = jnp.var(x, axis=axis, keepdims=True)
    return (x - m) / jnp.sqrt(v + eps)

def _scatter_add(tgt, idx, src, axis=0):
    return tgt.at[idx].add(src)

def _segment_sum(src, seg, n):
    return jax.ops.segment_sum(src, seg, n)
kernel_name = 'mk_adj_resnorm_d1_adj_r2_788ee5'

def setup_inputs(seed: int=0):
    np.random.seed(seed)
    _w = jnp.asarray

    def _rec_inputs():
        import jax
        import jax.numpy as jnp
        _gk = jax.random.key(seed)
        x = -0.0002422 + 1 * jax.random.normal(jax.random.fold_in(_gk, 1), (32, 256, 512), jnp.float32)
        _a = jax.random.bernoulli(jax.random.fold_in(_gk, 2), 0.0625, (32, 256, 256))
        adj = _a.astype(jnp.int32)
        return (x, adj)
    x, adj = _rec_inputs()

    def _L0_gnn_setup():
        import jax, jax.numpy as jnp
        import numpy as np
        IN_DIM = 512
        OUT_DIM = 512
        BATCH = 128
        NUM_OBJS = 100
        key = jax.random.key(seed)
        k1, k2, k3, k4, k5 = jax.random.split(key, 5)
        stdv = 1.0 / np.sqrt(OUT_DIM)
        feature = jax.random.normal(k1, (BATCH, NUM_OBJS, IN_DIM), dtype=jnp.float32)
        graph = jax.random.randint(k2, (BATCH, NUM_OBJS, NUM_OBJS), 0, 2, dtype=jnp.int32)
        weight = jax.random.uniform(k3, (IN_DIM, OUT_DIM), dtype=jnp.float32, minval=-stdv, maxval=stdv)
        wq = jax.random.uniform(k4, (IN_DIM, OUT_DIM), dtype=jnp.float32, minval=-stdv, maxval=stdv)
        wk = jax.random.uniform(k5, (IN_DIM, OUT_DIM), dtype=jnp.float32, minval=-stdv, maxval=stdv)
        return {'feature': feature, 'graph': graph, 'weight': weight, 'wq': wq, 'wk': wk}
    _L0_gnn_all = _L0_gnn_setup()
    _L0_gnn_in = {k: v for k, v in _L0_gnn_all.items() if k in ('weight', 'wq', 'wk')}
    del _L0_gnn_all
    return {'x': x, 'adj': adj, 'L0_gnn_weight': _L0_gnn_in['weight'], 'L0_gnn_wq': _L0_gnn_in['wq'], 'L0_gnn_wk': _L0_gnn_in['wk']}

def reference(x, adj, L0_gnn_weight, L0_gnn_wq, L0_gnn_wk):
    import jax
    import jax.numpy as jnp

    def _L0_gnn_ref(feature, graph, weight, wq, wk):
        import jax, jax.numpy as jnp
        import numpy as np
        IN_DIM = 512
        OUT_DIM = 512
        BATCH = 128
        NUM_OBJS = 100
        output = jnp.einsum('bni,io->bno', feature, weight)
        q = jnp.einsum('bni,io->bno', feature, wq)
        k = jnp.einsum('bni,io->bno', feature, wk)
        alpha = jnp.einsum('bno,bmo->bnm', q, k)
        alpha = jnp.maximum(alpha, 0.0) * (graph != 0).astype(alpha.dtype)
        alpha = jax.nn.softmax(alpha, axis=1)
        return jnp.einsum('bnm,bmo->bno', alpha, output)
    x = _layernorm(x + _L0_gnn_ref(x, adj, L0_gnn_weight, L0_gnn_wq, L0_gnn_wk), axis=-1)
    return x

_drawn_inputs = setup_inputs


def setup_inputs(seed=0):
    import zlib

    import numpy as np

    out = dict(_drawn_inputs(seed))
    spreads = {}
    factors = {}
    for name, (base, spread) in spreads.items():
        noise = np.random.default_rng([zlib.crc32(name.encode()), seed]).standard_normal(out[name].shape)
        drawn = base * np.exp(spread * noise) if base else spread * noise
        out[name] = jnp.asarray(drawn.astype(out[name].dtype))
    for name, factor in factors.items():
        out[name] = (out[name] * factor).astype(out[name].dtype)
    return out
```

```python
from contextlib import ExitStack

import concourse.bass as bass
from concourse import mybir

ALU = mybir.AluOpType
ACT = mybir.ActivationFunctionType
F32 = mybir.dt.float32
F32R = mybir.dt.float32r
I32 = mybir.dt.int32

P = 128
EPS = 1e-5


def gnn_resnorm(nc: bass.Bass, x, x_t, adj_t, w, wq_t, wk_t, out):
    B, N, D = x.shape
    PAIRS = B // 2
    K = D // P
    M = N // P
    R = 2 * M
    assert D == 512 and 2 * N == 512 and PAIRS % 2 == 0 and PAIRS >= 4 and K == R

    x_rows = x.rearrange("(a b) (t q) d -> a q (b t) d", b=2, q=P)
    out_rows = out.rearrange("(a b) (t q) d -> a q (b t) d", b=2, q=P)
    w_rows = w.rearrange("(k q) o -> q k o", q=P)
    wq_rows = wq_t.rearrange("(k q) j -> q k j", q=P)
    wk_rows = wk_t.rearrange("(k q) i -> q k i", q=P)

    with ExitStack() as ctx:
        def sb(name, shape, dt=F32):
            return ctx.enter_context(nc.sbuf_tensor(name, shape, dt))

        def bank(name):
            return ctx.enter_context(nc.psum_tensor(name, [P, 512], F32))

        def sem(name):
            return ctx.enter_context(nc.semaphore(name))

        xt = sb("xt", [P, 2, K, 2 * N])
        xt_hi = sb("xt_hi", [P, 2, K, 2 * N], F32R)
        xt_lo = sb("xt_lo", [P, 2, K, 2 * N], F32R)
        xn = sb("xn", [P, 2, R, D])
        adj = sb("adj", [P, 2, R, N], I32)
        y = sb("y", [P, 2, R, D])
        t_hi = sb("t_hi", [P, K, 2 * N], F32R)
        t_lo = sb("t_lo", [P, K, 2 * N], F32R)
        v_hi = sb("v_hi", [P, R, D], F32R)
        v_lo = sb("v_lo", [P, R, D], F32R)
        neg_scores = sb("neg_scores", [P, R, N])
        expd = sb("expd", [P, R, N])
        p_hi = sb("p_hi", [P, R, N], F32R)
        p_lo = sb("p_lo", [P, R, N], F32R)
        neg_max = sb("neg_max", [P, R])
        exp_sum = sb("exp_sum", [P, R])
        inv_sum = sb("inv_sum", [P, R])
        y_sum = sb("y_sum", [P, R])
        neg_mean = sb("neg_mean", [P, R])
        square_sum = sb("square_sum", [P, R])
        squares = sb("squares", [P, R, D])
        var_eps = sb("var_eps", [P, R])
        rstd = sb("rstd", [P, R])
        minus_half = sb("minus_half", [P, R])
        g_hi = sb("g_hi", [P, K, D], F32R)
        g_lo = sb("g_lo", [P, K, D], F32R)
        w_hi = sb("w_hi", [P, K, D], F32R)
        w_lo = sb("w_lo", [P, K, D], F32R)
        wk_hi = sb("wk_hi", [P, K, D], F32R)
        wk_lo = sb("wk_lo", [P, K, D], F32R)
        wk_raw = sb("wk_raw", [P, K, D])
        w_raw, wq_raw = y[:, 0], y[:, 1]
        wq_hi, wq_lo = t_hi, t_lo

        t_bank = [bank(f"t_bank{i}") for i in range(2)]
        o_bank = [bank(f"o_bank{i}") for i in range(2)]
        s_bank = [bank(f"s_bank{i}") for i in range(2)]
        v_bank = [bank(f"v_bank{i}") for i in range(2)]

        x0_loaded = [sem(f"x0_loaded{k}") for k in range(K)]
        w_loaded = [sem(f"w_loaded{k}") for k in range(K)]
        wq_loaded, wk_loaded = sem("wq_loaded"), sem("wk_loaded")
        xt_loaded = [sem(f"xt_loaded{s}") for s in range(2)]
        xn_loaded = [sem(f"xn_loaded{s}") for s in range(2)]
        adj_loaded = [sem(f"adj_loaded{s}") for s in range(2)]
        y_stored = [sem(f"y_stored{s}") for s in range(2)]
        w_hi_ready, w_lo_ready = sem("w_hi_ready"), sem("w_lo_ready")
        qk_hi_ready, qk_lo_ready = sem("qk_hi_ready"), sem("qk_lo_ready")
        g_filled, g_hi_ready, g_lo_ready = sem("g_filled"), sem("g_hi_ready"), sem("g_lo_ready")
        xt_hi_ready, xt_lo_ready = sem("xt_hi_ready"), sem("xt_lo_ready")
        t_filled, t_hi_ready, t_lo_ready = sem("t_filled"), sem("t_hi_ready"), sem("t_lo_ready")
        v_filled, v_hi_ready, v_lo_ready = sem("v_filled"), sem("v_hi_ready"), sem("v_lo_ready")
        s_filled, o_filled = sem("s_filled"), sem("o_filled")
        masked, max_ready, exp_ready = sem("masked"), sem("max_ready"), sem("exp_ready")
        inv_ready, p_hi_ready, p_lo_ready = sem("inv_ready"), sem("p_hi_ready"), sem("p_lo_ready")
        added, mean_ready, squared = sem("added"), sem("mean_ready"), sem("squared")
        half_ready, var_ready, rstd_ready, normed = (
            sem("half_ready"), sem("var_ready"), sem("rstd_ready"), sem("normed"))


        block = ctx.enter_context(nc.Block())

        @block.sync
        def _(sp):
            def load_xt(p, slot):
                sp.dma_start(xt[:, slot], x_t[p].rearrange("q (k n) -> q k n", k=K)).then_inc(xt_loaded[slot], 16)

            def load_adj(p, slot):
                sp.dma_start(adj[:, slot], adj_t[p].rearrange("q (r n) -> q r n", r=R)).then_inc(adj_loaded[slot], 16)

            def load_xn(p, slot):
                sp.dma_start(xn[:, slot], x_rows[p]).then_inc(xn_loaded[slot], 16)

            def store(p, slot):
                sp.wait_ge(normed, R * p + R)
                sp.dma_start(out_rows[p], y[:, slot]).then_inc(y_stored[slot], 16)

            def step(p, slot, turn, more=2):
                if more >= 2:
                    sp.wait_ge(xt_lo_ready, K * p + K)
                    load_xt(p + 2, slot)
                if more >= 1:
                    sp.wait_ge(added, R * p)
                    load_xn(p + 1, 1 - slot)
                if more >= 2:
                    sp.wait_ge(masked, 2 * p + 2)
                    load_adj(p + 2, slot)
                store(p - 1, 1 - slot)

            x0 = x_t[0].rearrange("q (k n) -> q k n", k=K)
            for k in range(K):
                sp.dma_start(xt[:, 0, k], x0[:, k]).then_inc(x0_loaded[k], 16)
                sp.dma_start(w_raw[:, k], w_rows[:, k]).then_inc(w_loaded[k], 16)
            sp.dma_start(wq_raw, wq_rows).then_inc(wq_loaded, 16)
            sp.dma_start(wk_raw[:], wk_rows).then_inc(wk_loaded, 16)
            load_adj(0, 0)
            load_xt(1, 1)
            load_xn(0, 0)
            load_adj(1, 1)
            sp.wait_ge(xt_lo_ready, K)
            load_xt(2, 0)
            load_xn(1, 1)
            sp.wait_ge(masked, 2)
            load_adj(2, 0)
            with sp.Fori(0, PAIRS // 2 - 2) as i:
                step(2 * i + 1, 1, i)
                step(2 * i + 2, 0, i + 1)
            for p in range(PAIRS - 3, PAIRS):
                step(p, p % 2, p // 2, more=PAIRS - 1 - p)
            store(PAIRS - 1, 1)
            for slot in range(2):
                sp.wait_ge(y_stored[slot], 16 * (PAIRS // 2))

        @block.tensor
        def _(pe):
            def product(dst, a, b, chunks, before=None):
                n = 0
                for k in range(chunks):
                    if before:
                        before(k)
                    for left, right in ((0, 0), (0, 1), (1, 0)):
                        last = nc.tensor.matmul(dst, a[left](k), b[right](k), start=(n == 0),
                                                stop=(n == 3 * chunks - 1))
                        n += 1
                return last

            def fill_g():
                for j in range(K):
                    if j >= 2:
                        pe.wait_ge(g_lo_ready, j - 1)
                    a = [lambda k, s=s: s[:, k, j * P:(j + 1) * P] for s in (wq_hi, wq_lo)]
                    b = [lambda k, s=s: s[:, k, :] for s in (wk_hi, wk_lo)]
                    before = (lambda k: pe.wait_ge(qk_lo_ready, 2 * k + 2)) if j == 0 else None
                    product(t_bank[j % 2][:], a, b, K, before).then_inc(g_filled, 1)

            def fill_t(p, slot, first=False):
                if first:
                    pe.wait_ge(g_lo_ready, K)
                pe.wait_ge(xt_lo_ready, K * p + K)
                for i in range(K):
                    if not (first and i < 2):
                        pe.wait_ge(t_lo_ready, K * p + i - 1)
                    a = [lambda k, s=s: s[:, k, i * P:(i + 1) * P] for s in (g_hi, g_lo)]
                    b = [lambda k, s=s: s[:, slot, k, :] for s in (xt_hi, xt_lo)]
                    product(t_bank[i % 2][:], a, b, K).then_inc(t_filled, 1)

            def fill_s(p, slot, first=False):
                pe.wait_ge(t_lo_ready, K * p + K)
                for g in range(2):
                    if not first:
                        pe.wait_ge(masked, 2 * p + g - 1)
                    for m in range(M):
                        at = g * N + m * P
                        a = [lambda k, s=s: s[:, slot, k, at:at + P] for s in (xt_hi, xt_lo)]
                        b = [lambda k, s=s: s[:, k, g * N:(g + 1) * N] for s in (t_hi, t_lo)]
                        last = product(s_bank[g][:, m * N:(m + 1) * N], a, b, K)
                    last.then_inc(s_filled, 1)

            def fill_v(p, slot, first=False):
                for r in range(R):
                    if not (first and r < 2):
                        pe.wait_ge(v_lo_ready, R * p + r - 1)
                    a = [lambda k, s=s: s[:, slot, k, r * P:(r + 1) * P] for s in (xt_hi, xt_lo)]
                    b = [lambda k, s=s: s[:, k, :] for s in (w_hi, w_lo)]

                    def split(k):
                        pe.wait_ge(xt_lo_ready, k + 1)
                        pe.wait_ge(w_lo_ready, k + 1)
                    product(v_bank[r % 2][:], a, b, K, split if first and r == 0 else None).then_inc(v_filled, 1)

            def fill_o(p, first=False):
                pe.wait_ge(v_lo_ready, R * p + R)
                pe.wait_ge(p_lo_ready, R * p + R)
                for r in range(R):
                    g, n = divmod(r, M)
                    if not (first and r < 2):
                        pe.wait_ge(added, R * p + r - 1)
                    a = [lambda m, s=s: s[:, g * M + m, n * P:(n + 1) * P] for s in (p_hi, p_lo)]
                    b = [lambda m, s=s: s[:, g * M + m, :] for s in (v_hi, v_lo)]
                    product(o_bank[r % 2][:], a, b, M).then_inc(o_filled, 1)

            def step(p, slot, turn, first=False):
                fill_t(p, slot)
                fill_o(p - 1, first)
                fill_s(p, slot)
                fill_v(p, slot)

            fill_v(0, 0, first=True)
            fill_g()
            fill_t(0, 0, first=True)
            fill_s(0, 0, first=True)
            step(1, 1, 0, first=True)
            step(2, 0, 1)
            with pe.Fori(1, PAIRS // 2 - 1) as i:
                step(2 * i + 1, 1, i)
                step(2 * i + 2, 0, i + 1)
            step(PAIRS - 1, 1, PAIRS // 2 - 1)
            fill_o(PAIRS - 1)

        @block.scalar
        def _(act):
            def split_x(p, slot, k):
                nc.scalar.copy(xt_hi[:, slot, k], xt[:, slot, k]).then_inc(xt_hi_ready, 1)

            def split_next_x(p, slot, turn, k):
                if k == 0:
                    act.wait_ge(xt_loaded[slot], 16 * turn + 16)
                    act.wait_ge(v_filled, R * p - R)
                split_x(p, slot, k)

            def split_v(p, r):
                act.wait_ge(v_filled, R * p + r + 1)
                nc.scalar.copy(v_hi[:, r], v_bank[r % 2][:]).then_inc(v_hi_ready, 1)

            def split_t(p, i):
                act.wait_ge(t_filled, K * p + i + 1)
                nc.scalar.copy(t_hi[:, i], t_bank[i % 2][:]).then_inc(t_hi_ready, 1)

            def exponent(p, r):
                act.wait_ge(max_ready, R * p + r + 1)
                nc.scalar.activation(expd[:, r], neg_scores[:, r], ACT.Exp, bias=neg_max[:, r:r + 1],
                                     scale=-1.0, accum_out=exp_sum[:, r:r + 1]).then_inc(exp_ready, 1)

            def split_p(p, r):
                if r == 0:
                    act.wait_ge(inv_ready, p + 1)
                nc.scalar.activation(p_hi[:, r], expd[:, r], ACT.Copy,
                                     scale=inv_sum[:, r:r + 1]).then_inc(p_hi_ready, 1)

            def centred_squares(p, slot, r):
                if r == 0:
                    act.wait_ge(mean_ready, p + 1)
                nc.scalar.activation(squares[:, r], y[:, slot, r], ACT.Square, bias=neg_mean[:, r:r + 1],
                                     accum_out=square_sum[:, r:r + 1]).then_inc(squared, 1)

            def step(p, slot, turn, more=True):
                for i in range(K):
                    split_t(p, i)
                    if more:
                        split_next_x(p + 1, 1 - slot, turn, i)
                for r in range(R):
                    centred_squares(p - 1, 1 - slot, r)
                exponent(p, 0)
                exponent(p, 1)
                split_v(p, 0)
                exponent(p, 2)
                exponent(p, 3)
                split_v(p, 1)
                split_p(p, 0)
                split_p(p, 1)
                split_v(p, 2)
                split_p(p, 2)
                split_p(p, 3)
                split_v(p, 3)

            for k in range(K):
                act.wait_ge(x0_loaded[k], 16)
                split_x(0, 0, k)
                act.wait_ge(w_loaded[k], 16)
                nc.scalar.copy(w_hi[:, k], w_raw[:, k]).then_inc(w_hi_ready, 1)
            act.wait_ge(wq_loaded, 16)
            act.wait_ge(wk_loaded, 16)
            for k in range(K):
                nc.scalar.copy(wq_hi[:, k], wq_raw[:, k]).then_inc(qk_hi_ready, 1)
                nc.scalar.copy(wk_hi[:, k], wk_raw[:, k]).then_inc(qk_hi_ready, 1)
                split_v(0, k)
            for j in range(K):
                act.wait_ge(g_filled, j + 1)
                nc.scalar.mul(g_hi[:, j], t_bank[j % 2][:], -1.0).then_inc(g_hi_ready, 1)
            for i in range(K):
                split_t(0, i)
                if i == 0:
                    act.wait_ge(xt_loaded[1], 16)
                split_x(1, 1, i)
            for r in range(R):
                exponent(0, r)
            for r in range(R):
                split_p(0, r)
            with act.Fori(0, PAIRS // 2 - 1) as i:
                step(2 * i + 1, 1, i)
                step(2 * i + 2, 0, i + 1)
            step(PAIRS - 1, 1, PAIRS // 2 - 1, more=False)
            for r in range(R):
                centred_squares(PAIRS - 1, 1, r)

        @block.vector
        def _(dve):
            def rest(dst, whole, hi):
                return nc.vector.tensor_tensor(dst, whole, hi.bitcast(F32), ALU.subtract)

            def split_x(p, slot, k):
                dve.wait_ge(xt_hi_ready, K * p + k + 1)
                rest(xt_lo[:, slot, k], xt[:, slot, k], xt_hi[:, slot, k]).then_inc(xt_lo_ready, 1)

            def split_t(p, i):
                dve.wait_ge(t_hi_ready, K * p + i + 1)
                rest(t_lo[:, i], t_bank[i % 2][:], t_hi[:, i]).then_inc(t_lo_ready, 1)

            def split_v(p, r):
                dve.wait_ge(v_hi_ready, R * p + r + 1)
                rest(v_lo[:, r], v_bank[r % 2][:], v_hi[:, r]).then_inc(v_lo_ready, 1)

            def mask(p, slot, turn, g):
                if g == 0:
                    dve.wait_ge(adj_loaded[slot], 16 * turn + 16)
                dve.wait_ge(s_filled, 2 * p + g + 1)
                nc.vector.scalar_tensor_tensor(
                    out=neg_scores[:, g * M:(g + 1) * M], in0=adj[:, slot, g * M:(g + 1) * M], scalar=0.0,
                    in1=s_bank[g][:].rearrange("q (m n) -> q m n", m=M), op0=ALU.not_equal,
                    op1=ALU.mult).then_inc(masked, 1)

            def relu_max(p, r):
                dve.wait_ge(masked, 2 * p + r // M + 1)
                nc.vector.tensor_scalar(neg_scores[:, r], neg_scores[:, r], 0.0, None, ALU.min, ALU.min,
                                        accum_out=neg_max[:, r:r + 1]).then_inc(max_ready, 1)

            def invert(p):
                dve.wait_ge(exp_ready, R * p + R)
                nc.vector.reciprocal(inv_sum[:], exp_sum[:]).then_inc(inv_ready, 1)

            def split_p(p, r):
                if r == 0:
                    dve.wait_ge(inv_ready, p + 1)
                dve.wait_ge(p_hi_ready, R * p + r + 1)
                nc.vector.scalar_tensor_tensor(
                    out=p_lo[:, r], in0=expd[:, r], scalar=inv_sum[:, r:r + 1],
                    in1=p_hi[:, r].bitcast(F32), op0=ALU.mult, op1=ALU.subtract).then_inc(p_lo_ready, 1)

            def residual(p, slot, turn, r, first):
                if r == 0:
                    dve.wait_ge(xn_loaded[slot], 16 * turn + 16)
                    if not first:
                        dve.wait_ge(y_stored[slot], 16 * turn)
                dve.wait_ge(o_filled, R * p + r + 1)
                nc.vector.scalar_tensor_tensor(
                    out=y[:, slot, r], in0=o_bank[r % 2][:], scalar=1.0, in1=xn[:, slot, r], op0=ALU.mult,
                    op1=ALU.add, accum_out=y_sum[:, r:r + 1]).then_inc(added, 1)

            def means(p):
                dve.wait_ge(added, R * p + R)
                nc.vector.tensor_scalar_mul(neg_mean[:], y_sum[:], -1.0 / D).then_inc(mean_ready, 1)

            def variances(p):
                dve.wait_ge(squared, R * p + R)
                nc.vector.tensor_scalar(var_eps[:], square_sum[:], 1.0 / D, EPS, ALU.mult,
                                        ALU.add).then_inc(var_ready, 1)

            def normalise(p, slot, r):
                if r == 0:
                    dve.wait_ge(rstd_ready, p + 1)
                nc.vector.tensor_scalar(y[:, slot, r], y[:, slot, r], neg_mean[:, r:r + 1], rstd[:, r:r + 1],
                                        ALU.add, ALU.mult).then_inc(normed, 1)

            def finish(p, slot, turn, first=False):
                for r in range(R):
                    residual(p, slot, turn, r, first)
                means(p)

            def step(p, slot, turn, first=False, more=True):
                before = turn if slot == 1 else turn - 1
                for i in range(K):
                    split_t(p, i)
                    if more:
                        split_x(p + 1, 1 - slot, i)
                finish(p - 1, 1 - slot, before, first)
                mask(p, slot, turn, 0)
                relu_max(p, 0)
                relu_max(p, 1)
                mask(p, slot, turn, 1)
                relu_max(p, 2)
                relu_max(p, 3)
                variances(p - 1)
                split_v(p, 0)
                normalise(p - 1, 1 - slot, 0)
                normalise(p - 1, 1 - slot, 1)
                split_v(p, 1)
                invert(p)
                normalise(p - 1, 1 - slot, 2)
                normalise(p - 1, 1 - slot, 3)
                split_v(p, 2)
                split_p(p, 0)
                split_p(p, 1)
                split_v(p, 3)
                split_p(p, 2)
                split_p(p, 3)

            for k in range(K):
                split_x(0, 0, k)
                dve.wait_ge(w_hi_ready, k + 1)
                rest(w_lo[:, k], w_raw[:, k], w_hi[:, k]).then_inc(w_lo_ready, 1)
            for k in range(K):
                dve.wait_ge(qk_hi_ready, 2 * k + 2)
                rest(wq_lo[:, k], wq_raw[:, k], wq_hi[:, k]).then_inc(qk_lo_ready, 1)
                rest(wk_lo[:, k], wk_raw[:, k], wk_hi[:, k]).then_inc(qk_lo_ready, 1)
                split_v(0, k)
            for j in range(K):
                dve.wait_ge(g_hi_ready, j + 1)
                nc.vector.scalar_tensor_tensor(
                    out=g_lo[:, j], in0=t_bank[j % 2][:], scalar=-1.0, in1=g_hi[:, j].bitcast(F32),
                    op0=ALU.mult, op1=ALU.subtract).then_inc(g_lo_ready, 1)
            for i in range(K):
                split_t(0, i)
                split_x(1, 1, i)
            for g in range(2):
                mask(0, 0, 0, g)
                for r in range(g * M, (g + 1) * M):
                    relu_max(0, r)
            invert(0)
            for r in range(R):
                split_p(0, r)
            step(1, 1, 0, first=True)
            step(2, 0, 1, first=True)
            with dve.Fori(1, PAIRS // 2 - 1) as i:
                step(2 * i + 1, 1, i)
                step(2 * i + 2, 0, i + 1)
            step(PAIRS - 1, 1, PAIRS // 2 - 1, more=False)
            finish(PAIRS - 1, 1, PAIRS // 2 - 1)
            variances(PAIRS - 1)
            for r in range(R):
                normalise(PAIRS - 1, 1, r)

        @block.gpsimd
        def _(pool):
            nc.gpsimd.memset(minus_half[:], -0.5).then_inc(half_ready, 1)
            pool.wait_ge(half_ready, 1)
            with pool.Fori(0, PAIRS) as p:
                pool.wait_ge(var_ready, p + 1)
                nc.gpsimd.tensor_tensor(rstd[:], var_eps[:], minus_half[:], ALU.pow).then_inc(rstd_ready, 1)


def kernel(x, adj, L0_gnn_weight, L0_gnn_wq, L0_gnn_wk):
    import numpy as np
    from concourse import bacc
    from concourse.bass_utils import run_bass_kernel_spmd

    x, adj = np.asarray(x), np.asarray(adj)
    B, N, D = x.shape
    arrays = {
        "x": np.ascontiguousarray(x),
        "x_t": np.ascontiguousarray(
            x.reshape(B // 2, 2, N, D // P, P).transpose(0, 4, 3, 1, 2)).reshape(B // 2, P, -1),
        "adj_t": np.ascontiguousarray(
            adj.reshape(B // 2, 2, N, N // P, P).transpose(0, 4, 1, 3, 2)).reshape(B // 2, P, -1),
        "w": np.ascontiguousarray(L0_gnn_weight),
        "wq_t": np.ascontiguousarray(np.asarray(L0_gnn_wq).T),
        "wk_t": np.ascontiguousarray(np.asarray(L0_gnn_wk).T),
    }
    nc = bacc.Bacc("TRN2", target_bir_lowering=False, num_devices=1)
    args = [nc.dram_tensor(f"in_{name}", a.shape, mybir.dt.from_np(a.dtype), kind="ExternalInput").ap()
            for name, a in arrays.items()]
    out = nc.dram_tensor("out", x.shape, F32, kind="ExternalOutput").ap()
    gnn_resnorm(nc, *args, out)
    r = run_bass_kernel_spmd(nc, [{f"in_{name}": a for name, a in arrays.items()}], core_ids=[0])
    return r.results[0]["out"]
```

```python
from contextlib import ExitStack

import concourse.bass as bass
from concourse import mybir

ALU = mybir.AluOpType
ACT = mybir.ActivationFunctionType
F32 = mybir.dt.float32
F32R = mybir.dt.float32r
I32 = mybir.dt.int32

P = 128
EPS = 1e-5


def gnn_resnorm(nc: bass.Bass, x, x_t, adj_t, w, wq_t, wk_t, out):
    B, N, D = x.shape
    PAIRS = B // 2
    K = D // P
    M = N // P
    R = 2 * M
    assert D == 512 and 2 * N == 512 and PAIRS % 2 == 0 and PAIRS >= 4 and K == R

    x_rows = x.rearrange("(a b) (t q) d -> a q (b t) d", b=2, q=P)
    out_rows = out.rearrange("(a b) (t q) d -> a q (b t) d", b=2, q=P)
    w_rows = w.rearrange("(k q) o -> q k o", q=P)
    wq_rows = wq_t.rearrange("(k q) j -> q k j", q=P)
    wk_rows = wk_t.rearrange("(k q) i -> q k i", q=P)

    with ExitStack() as ctx:
        def sb(name, shape, dt=F32):
            return ctx.enter_context(nc.sbuf_tensor(name, shape, dt))

        def bank(name):
            return ctx.enter_context(nc.psum_tensor(name, [P, 512], F32))

        def sem(name):
            return ctx.enter_context(nc.semaphore(name))

        xt = sb("xt", [P, 2, K, 2 * N])
        xt_hi = sb("xt_hi", [P, 2, K, 2 * N], F32R)
        xt_lo = sb("xt_lo", [P, 2, K, 2 * N], F32R)
        xn = sb("xn", [P, 2, R, D])
        adj = sb("adj", [P, 2, R, N], I32)
        y = sb("y", [P, 2, R, D])
        t_hi = sb("t_hi", [P, K, 2 * N], F32R)
        t_lo = sb("t_lo", [P, K, 2 * N], F32R)
        v_hi = sb("v_hi", [P, R, D], F32R)
        v_lo = sb("v_lo", [P, R, D], F32R)
        neg_scores = sb("neg_scores", [P, R, N])
        expd = sb("expd", [P, R, N])
        p_hi = sb("p_hi", [P, R, N], F32R)
        p_lo = sb("p_lo", [P, R, N], F32R)
        neg_max = sb("neg_max", [P, R])
        exp_sum = sb("exp_sum", [P, R])
        inv_sum = sb("inv_sum", [P, R])
        y_sum = sb("y_sum", [P, R])
        neg_mean = sb("neg_mean", [P, R])
        square_sum = sb("square_sum", [P, R])
        squares = sb("squares", [P, R, D])
        var_eps = sb("var_eps", [P, R])
        rstd = sb("rstd", [P, R])
        minus_half = sb("minus_half", [P, R])
        g_hi = sb("g_hi", [P, K, D], F32R)
        g_lo = sb("g_lo", [P, K, D], F32R)
        w_hi = sb("w_hi", [P, K, D], F32R)
        w_lo = sb("w_lo", [P, K, D], F32R)
        wk_hi = sb("wk_hi", [P, K, D], F32R)
        wk_lo = sb("wk_lo", [P, K, D], F32R)
        wk_raw = sb("wk_raw", [P, K, D])
        w_raw, wq_raw = y[:, 0], y[:, 1]
        wq_hi, wq_lo = t_hi, t_lo

        t_bank = [bank(f"t_bank{i}") for i in range(2)]
        o_bank = [bank(f"o_bank{i}") for i in range(2)]
        s_bank = [bank(f"s_bank{i}") for i in range(2)]
        v_bank = [bank(f"v_bank{i}") for i in range(2)]
        v0_bank, g_bank = v_bank + t_bank, s_bank + o_bank

        x0_loaded = [sem(f"x0_loaded{k}") for k in range(K)]
        w_loaded = [sem(f"w_loaded{k}") for k in range(K)]
        wq_loaded, wk_loaded = sem("wq_loaded"), sem("wk_loaded")
        xt_loaded = [sem(f"xt_loaded{s}") for s in range(2)]
        xn_loaded = [sem(f"xn_loaded{s}") for s in range(2)]
        adj_loaded = [sem(f"adj_loaded{s}") for s in range(2)]
        y_stored = [sem(f"y_stored{s}") for s in range(2)]
        w_hi_ready, w_lo_ready = sem("w_hi_ready"), sem("w_lo_ready")
        qk_hi_ready, qk_lo_ready = sem("qk_hi_ready"), sem("qk_lo_ready")
        g_filled, g_hi_ready, g_lo_ready = sem("g_filled"), sem("g_hi_ready"), sem("g_lo_ready")
        xt_hi_ready, xt_lo_ready = sem("xt_hi_ready"), sem("xt_lo_ready")
        t_filled, t_hi_ready, t_lo_ready = sem("t_filled"), sem("t_hi_ready"), sem("t_lo_ready")
        v_filled, v_hi_ready, v_lo_ready = sem("v_filled"), sem("v_hi_ready"), sem("v_lo_ready")
        s_filled, o_filled = sem("s_filled"), sem("o_filled")
        masked, max_ready, exp_ready = sem("masked"), sem("max_ready"), sem("exp_ready")
        inv_ready, p_hi_ready, p_lo_ready = sem("inv_ready"), sem("p_hi_ready"), sem("p_lo_ready")
        added, mean_ready, squared = sem("added"), sem("mean_ready"), sem("squared")
        half_ready, var_ready, rstd_ready, normed = (
            sem("half_ready"), sem("var_ready"), sem("rstd_ready"), sem("normed"))


        x_chunks = [(0,), (1, 2), (3,), ()]

        block = ctx.enter_context(nc.Block())

        @block.sync
        def _(sp):
            def load_xt(p, slot):
                sp.dma_start(xt[:, slot], x_t[p].rearrange("q (k n) -> q k n", k=K)).then_inc(xt_loaded[slot], 16)

            def load_adj(p, slot):
                sp.dma_start(adj[:, slot], adj_t[p].rearrange("q (r n) -> q r n", r=R)).then_inc(adj_loaded[slot], 16)

            def load_xn(p, slot):
                sp.dma_start(xn[:, slot], x_rows[p]).then_inc(xn_loaded[slot], 16)

            def store(p, slot):
                sp.wait_ge(normed, R * p + R)
                sp.dma_start(out_rows[p], y[:, slot]).then_inc(y_stored[slot], 16)

            def step(p, slot, more=2):
                if more >= 2:
                    sp.wait_ge(xt_lo_ready, K * p + K)
                    load_xt(p + 2, slot)
                if more >= 1:
                    sp.wait_ge(added, R * p)
                    load_xn(p + 1, 1 - slot)
                if more >= 2:
                    sp.wait_ge(masked, 2 * p + 2)
                    load_adj(p + 2, slot)
                store(p - 1, 1 - slot)

            x0 = x_t[0].rearrange("q (k n) -> q k n", k=K)
            for k in range(K):
                sp.dma_start(xt[:, 0, k], x0[:, k]).then_inc(x0_loaded[k], 16)
                sp.dma_start(w_raw[:, k], w_rows[:, k]).then_inc(w_loaded[k], 16)
            sp.dma_start(wq_raw, wq_rows).then_inc(wq_loaded, 16)
            sp.dma_start(wk_raw[:], wk_rows).then_inc(wk_loaded, 16)
            load_xt(1, 1)
            load_adj(0, 0)
            load_xn(0, 0)
            load_adj(1, 1)
            sp.wait_ge(xt_lo_ready, K)
            load_xt(2, 0)
            load_xn(1, 1)
            sp.wait_ge(masked, 2)
            load_adj(2, 0)
            with sp.Fori(0, PAIRS // 2 - 2) as i:
                step(2 * i + 1, 1)
                step(2 * i + 2, 0)
            for p in range(PAIRS - 3, PAIRS):
                step(p, p % 2, more=PAIRS - 1 - p)
            for r in range(R):
                sp.wait_ge(normed, R * (PAIRS - 1) + r + 1)
                sp.dma_start(out_rows[PAIRS - 1][:, r], y[:, 1, r]).then_inc(y_stored[1], 16)
            sp.wait_ge(y_stored[0], 16 * (PAIRS // 2))
            sp.wait_ge(y_stored[1], 16 * (PAIRS // 2 - 1 + R))

        @block.tensor
        def _(pe):
            def add_chunk(dst, a, b, first, last):
                nc.tensor.matmul(dst, a[0], b[0], start=first, stop=False)
                nc.tensor.matmul(dst, a[0], b[1], start=False, stop=False)
                return nc.tensor.matmul(dst, a[1], b[0], start=False, stop=last)

            def g_chunk(j, k):
                cols = slice(j * P, (j + 1) * P)
                return add_chunk(g_bank[j][:], (wq_hi[:, k, cols], wq_lo[:, k, cols]),
                                 (wk_hi[:, k], wk_lo[:, k]), k == 0, k == K - 1)

            def t_chunk(i, k, slot):
                cols = slice(i * P, (i + 1) * P)
                return add_chunk(t_bank[i % 2][:], (g_hi[:, k, cols], g_lo[:, k, cols]),
                                 (xt_hi[:, slot, k], xt_lo[:, slot, k]), k == 0, k == K - 1)

            def s_chunk(g, m, k, slot):
                rows, cols = slice(g * N + m * P, g * N + (m + 1) * P), slice(g * N, (g + 1) * N)
                return add_chunk(s_bank[g][:, m * N:(m + 1) * N],
                                 (xt_hi[:, slot, k, rows], xt_lo[:, slot, k, rows]),
                                 (t_hi[:, k, cols], t_lo[:, k, cols]), k == 0, k == K - 1)

            def v_chunk(r, k, slot):
                rows = slice(r * P, (r + 1) * P)
                return add_chunk(v_bank[r % 2][:], (xt_hi[:, slot, k, rows], xt_lo[:, slot, k, rows]),
                                 (w_hi[:, k], w_lo[:, k]), k == 0, k == K - 1)

            def o_chunk(g, n, m):
                rows, t = slice(n * P, (n + 1) * P), g * M + m
                return add_chunk(o_bank[n % 2][:], (p_hi[:, t, rows], p_lo[:, t, rows]),
                                 (v_hi[:, t], v_lo[:, t]), m == 0, m == M - 1)

            def fill_first_v():
                for k in range(K):
                    for parts, x_ready, w_ready in (
                            (((xt_hi, w_hi),), xt_hi_ready, w_hi_ready),
                            (((xt_hi, w_lo), (xt_lo, w_hi)), xt_lo_ready, w_lo_ready)):
                        pe.wait_ge(x_ready, k + 1)
                        pe.wait_ge(w_ready, k + 1)
                        for r in range(R):
                            for left, right in parts:
                                last = nc.tensor.matmul(
                                    v0_bank[r][:], left[:, 0, k, r * P:(r + 1) * P], right[:, k],
                                    start=(k == 0 and right is w_hi and left is xt_hi),
                                    stop=(k == K - 1 and left is xt_lo))
                            if k == K - 1 and left is xt_lo:
                                last.then_inc(v_filled, 1)

            def fill_g():
                for k in range(K):
                    pe.wait_ge(qk_lo_ready, 2 * k + 2)
                    for j in range(2):
                        last = g_chunk(j, k)
                        if k == K - 1:
                            last.then_inc(g_filled, 1)
                for j in range(2, K):
                    for k in range(K):
                        last = g_chunk(j, k)
                    last.then_inc(g_filled, 1)


            def fill_t(p, slot, first=False):
                if not first:
                    pe.wait_ge(xt_lo_ready, K * p + K)
                for i in range(K):
                    if i >= 2:
                        pe.wait_ge(t_lo_ready, K * p + i - 1)
                    for k in range(K):
                        if first and i == 0:
                            pe.wait_ge(g_lo_ready, k + 1)
                        last = t_chunk(i, k, slot)
                    last.then_inc(t_filled, 1)

            def fill_s(p, slot, first=False):
                if not first:
                    pe.wait_ge(t_lo_ready, K * p + K)
                for g in range(2):
                    for m in range(M):
                        for k in range(K):
                            if first and g == 0 and m == 0:
                                pe.wait_ge(t_lo_ready, k + 1)
                            last = s_chunk(g, m, k, slot)
                    last.then_inc(s_filled, 1)

            def fill_v(p, slot):
                for r in range(R):
                    pe.wait_ge(v_lo_ready, R * p + r - 1)
                    for k in range(K):
                        last = v_chunk(r, k, slot)
                    last.then_inc(v_filled, 1)

            def fill_o(p, first=False):
                for g in range(2):
                    if first and g == 0:
                        pe.wait_ge(p_lo_ready, R)
                    elif g == 0:
                        pe.wait_ge(p_lo_ready, R * p + M)
                    elif not first:
                        pe.wait_ge(v_lo_ready, R * p + R)
                    for n in range(M):
                        if g == 1:
                            pe.wait_ge(added, R * p + g * M + n - 1)
                        for m in range(M):
                            last = o_chunk(g, n, m)
                        last.then_inc(o_filled, 1)

            def step(p, slot, first=False):
                fill_t(p, slot)
                fill_o(p - 1, first)
                fill_s(p, slot)
                fill_v(p, slot)

            fill_first_v()
            fill_g()
            fill_t(0, 0, first=True)
            fill_s(0, 0, first=True)
            step(1, 1, first=True)
            step(2, 0)
            with pe.Fori(1, PAIRS // 2 - 1) as i:
                step(2 * i + 1, 1)
                step(2 * i + 2, 0)
            step(PAIRS - 1, 1)
            fill_o(PAIRS - 1)

        @block.scalar
        def _(act):
            def split_x(p, slot, k):
                nc.scalar.copy(xt_hi[:, slot, k], xt[:, slot, k]).then_inc(xt_hi_ready, 1)

            def split_next_x(p, slot, turn, k):
                if k == 0:
                    act.wait_ge(xt_loaded[slot], 16 * turn + 16)
                    act.wait_ge(v_filled, R * p - R)
                split_x(p, slot, k)

            def split_v(p, r, banks=2 * v_bank):
                act.wait_ge(v_filled, R * p + r + 1)
                nc.scalar.copy(v_hi[:, r], banks[r][:]).then_inc(v_hi_ready, 1)

            def split_t(p, i):
                act.wait_ge(t_filled, K * p + i + 1)
                nc.scalar.copy(t_hi[:, i], t_bank[i % 2][:]).then_inc(t_hi_ready, 1)

            def exponent(p, r):
                act.wait_ge(max_ready, R * p + r + 1)
                nc.scalar.activation(expd[:, r], neg_scores[:, r], ACT.Exp, bias=neg_max[:, r:r + 1],
                                     scale=-1.0, accum_out=exp_sum[:, r:r + 1]).then_inc(exp_ready, 1)

            def split_p(p, r):
                if r == 0:
                    act.wait_ge(inv_ready, p + 1)
                nc.scalar.activation(p_hi[:, r], expd[:, r], ACT.Copy,
                                     scale=inv_sum[:, r:r + 1]).then_inc(p_hi_ready, 1)

            def centred_squares(p, slot, r, by_tile=False):
                if by_tile:
                    act.wait_ge(mean_ready, p + 1 + r)
                elif r == 0:
                    act.wait_ge(mean_ready, p + 1)
                nc.scalar.activation(squares[:, r], y[:, slot, r], ACT.Square, bias=neg_mean[:, r:r + 1],
                                     accum_out=square_sum[:, r:r + 1]).then_inc(squared, 1)

            def step(p, slot, turn, more=True, softmax_0=False):
                for i in range(K):
                    split_t(p, i)
                    if softmax_0 and i == 0:
                        for r in range(R):
                            split_p(0, r)
                    if more:
                        for k in x_chunks[i]:
                            split_next_x(p + 1, 1 - slot, turn, k)
                for r in range(R):
                    centred_squares(p - 1, 1 - slot, r)
                exponent(p, 0)
                exponent(p, 1)
                split_v(p, 0)
                exponent(p, 2)
                exponent(p, 3)
                split_v(p, 1)
                split_p(p, 0)
                split_p(p, 1)
                split_v(p, 2)
                split_p(p, 2)
                split_p(p, 3)
                split_v(p, 3)

            for k in range(K):
                act.wait_ge(x0_loaded[k], 16)
                split_x(0, 0, k)
                act.wait_ge(w_loaded[k], 16)
                nc.scalar.copy(w_hi[:, k], w_raw[:, k]).then_inc(w_hi_ready, 1)
            act.wait_ge(wq_loaded, 16)
            act.wait_ge(wk_loaded, 16)
            for k in range(K):
                nc.scalar.copy(wq_hi[:, k], wq_raw[:, k]).then_inc(qk_hi_ready, 1)
                nc.scalar.copy(wk_hi[:, k], wk_raw[:, k]).then_inc(qk_hi_ready, 1)
            for r in range(R):
                split_v(0, r, v0_bank)
            for j in range(K):
                act.wait_ge(g_filled, j + 1)
                nc.scalar.mul(g_hi[:, j], g_bank[j][:], -1.0).then_inc(g_hi_ready, 1)
            for i in range(K):
                split_t(0, i)
                if i == 0:
                    act.wait_ge(xt_loaded[1], 16)
                split_x(1, 1, i)
            for r in range(R):
                exponent(0, r)
            step(1, 1, 0, softmax_0=True)
            step(2, 0, 1)
            with act.Fori(1, PAIRS // 2 - 1) as i:
                step(2 * i + 1, 1, i)
                step(2 * i + 2, 0, i + 1)
            step(PAIRS - 1, 1, PAIRS // 2 - 1, more=False)
            for r in range(R):
                centred_squares(PAIRS - 1, 1, r, by_tile=True)

        @block.vector
        def _(dve):
            def rest(dst, whole, hi):
                return nc.vector.tensor_tensor(dst, whole, hi.bitcast(F32), ALU.subtract)

            def split_x(p, slot, k):
                dve.wait_ge(xt_hi_ready, K * p + k + 1)
                rest(xt_lo[:, slot, k], xt[:, slot, k], xt_hi[:, slot, k]).then_inc(xt_lo_ready, 1)

            def split_t(p, i):
                dve.wait_ge(t_hi_ready, K * p + i + 1)
                rest(t_lo[:, i], t_bank[i % 2][:], t_hi[:, i]).then_inc(t_lo_ready, 1)

            def split_v(p, r, banks=2 * v_bank):
                dve.wait_ge(v_hi_ready, R * p + r + 1)
                rest(v_lo[:, r], banks[r][:], v_hi[:, r]).then_inc(v_lo_ready, 1)

            def mask(p, slot, turn, g):
                if g == 0:
                    dve.wait_ge(adj_loaded[slot], 16 * turn + 16)
                dve.wait_ge(s_filled, 2 * p + g + 1)
                nc.vector.scalar_tensor_tensor(
                    out=neg_scores[:, g * M:(g + 1) * M], in0=adj[:, slot, g * M:(g + 1) * M], scalar=0.0,
                    in1=s_bank[g][:].rearrange("q (m n) -> q m n", m=M), op0=ALU.not_equal,
                    op1=ALU.mult).then_inc(masked, 1)

            def relu_max(p, r):
                dve.wait_ge(masked, 2 * p + r // M + 1)
                nc.vector.tensor_scalar(neg_scores[:, r], neg_scores[:, r], 0.0, None, ALU.min, ALU.min,
                                        accum_out=neg_max[:, r:r + 1]).then_inc(max_ready, 1)

            def invert(p):
                dve.wait_ge(exp_ready, R * p + R)
                nc.vector.reciprocal(inv_sum[:], exp_sum[:]).then_inc(inv_ready, 1)

            def split_p(p, r):
                if r == 0:
                    dve.wait_ge(inv_ready, p + 1)
                dve.wait_ge(p_hi_ready, R * p + r + 1)
                nc.vector.scalar_tensor_tensor(
                    out=p_lo[:, r], in0=expd[:, r], scalar=inv_sum[:, r:r + 1],
                    in1=p_hi[:, r].bitcast(F32), op0=ALU.mult, op1=ALU.subtract).then_inc(p_lo_ready, 1)

            def residual(p, slot, turn, r, first):
                if r == 0:
                    dve.wait_ge(xn_loaded[slot], 16 * turn + 16)
                    if not first:
                        dve.wait_ge(y_stored[slot], 16 * turn)
                dve.wait_ge(o_filled, R * p + r + 1)
                nc.vector.scalar_tensor_tensor(
                    out=y[:, slot, r], in0=o_bank[r % 2][:], scalar=1.0, in1=xn[:, slot, r], op0=ALU.mult,
                    op1=ALU.add, accum_out=y_sum[:, r:r + 1]).then_inc(added, 1)

            def means(p):
                dve.wait_ge(added, R * p + R)
                nc.vector.tensor_scalar_mul(neg_mean[:], y_sum[:], -1.0 / D).then_inc(mean_ready, 1)

            def variances(p):
                dve.wait_ge(squared, R * p + R)
                nc.vector.tensor_scalar(var_eps[:], square_sum[:], 1.0 / D, EPS, ALU.mult,
                                        ALU.add).then_inc(var_ready, 1)

            def normalise(p, slot, r):
                if r == 0:
                    dve.wait_ge(rstd_ready, p + 1)
                nc.vector.tensor_scalar(y[:, slot, r], y[:, slot, r], neg_mean[:, r:r + 1], rstd[:, r:r + 1],
                                        ALU.add, ALU.mult).then_inc(normed, 1)

            def finish(p, slot, turn, first=False):
                for r in range(R):
                    residual(p, slot, turn, r, first)
                means(p)

            def step(p, slot, turn, first=False, more=True, softmax_0=False):
                before = turn if slot == 1 else turn - 1
                for i in range(K):
                    split_t(p, i)
                    if softmax_0 and i == 0:
                        invert(0)
                        for r in range(R):
                            split_p(0, r)
                    if more:
                        for k in x_chunks[i]:
                            split_x(p + 1, 1 - slot, k)
                finish(p - 1, 1 - slot, before, first)
                mask(p, slot, turn, 0)
                relu_max(p, 0)
                relu_max(p, 1)
                mask(p, slot, turn, 1)
                relu_max(p, 2)
                relu_max(p, 3)
                variances(p - 1)
                split_v(p, 0)
                normalise(p - 1, 1 - slot, 0)
                normalise(p - 1, 1 - slot, 1)
                split_v(p, 1)
                invert(p)
                normalise(p - 1, 1 - slot, 2)
                normalise(p - 1, 1 - slot, 3)
                split_v(p, 2)
                for r in range(R):
                    split_p(p, r)
                split_v(p, 3)

            for k in range(K):
                split_x(0, 0, k)
                dve.wait_ge(w_hi_ready, k + 1)
                rest(w_lo[:, k], w_raw[:, k], w_hi[:, k]).then_inc(w_lo_ready, 1)
            for k in range(K):
                dve.wait_ge(qk_hi_ready, 2 * k + 2)
                rest(wq_lo[:, k], wq_raw[:, k], wq_hi[:, k]).then_inc(qk_lo_ready, 1)
                rest(wk_lo[:, k], wk_raw[:, k], wk_hi[:, k]).then_inc(qk_lo_ready, 1)
            for r in range(R):
                split_v(0, r, v0_bank)
            for j in range(K):
                dve.wait_ge(g_hi_ready, j + 1)
                nc.vector.scalar_tensor_tensor(
                    out=g_lo[:, j], in0=g_bank[j][:], scalar=-1.0, in1=g_hi[:, j].bitcast(F32),
                    op0=ALU.mult, op1=ALU.subtract).then_inc(g_lo_ready, 1)
            for i in range(K):
                split_t(0, i)
                split_x(1, 1, i)
            for g in range(2):
                mask(0, 0, 0, g)
                for r in range(g * M, (g + 1) * M):
                    relu_max(0, r)
            step(1, 1, 0, first=True, softmax_0=True)
            step(2, 0, 1, first=True)
            with dve.Fori(1, PAIRS // 2 - 1) as i:
                step(2 * i + 1, 1, i)
                step(2 * i + 2, 0, i + 1)
            step(PAIRS - 1, 1, PAIRS // 2 - 1, more=False)

            def mean_of(r):
                dve.wait_ge(added, R * (PAIRS - 1) + r + 1)
                nc.vector.tensor_scalar_mul(neg_mean[:, r:r + 1], y_sum[:, r:r + 1],
                                            -1.0 / D).then_inc(mean_ready, 1)

            def variance_of(r):
                dve.wait_ge(squared, R * (PAIRS - 1) + r + 1)
                nc.vector.tensor_scalar(var_eps[:, r:r + 1], square_sum[:, r:r + 1], 1.0 / D, EPS, ALU.mult,
                                        ALU.add).then_inc(var_ready, 1)

            def normalise_last(r):
                dve.wait_ge(rstd_ready, PAIRS + r)
                nc.vector.tensor_scalar(y[:, 1, r], y[:, 1, r], neg_mean[:, r:r + 1], rstd[:, r:r + 1],
                                        ALU.add, ALU.mult).then_inc(normed, 1)

            for r in range(R):
                residual(PAIRS - 1, 1, PAIRS // 2 - 1, r, False)
                mean_of(r)
                if r >= 1:
                    variance_of(r - 1)
                if r >= 2:
                    normalise_last(r - 2)
            variance_of(R - 1)
            normalise_last(R - 2)
            normalise_last(R - 1)

        @block.gpsimd
        def _(pool):
            nc.gpsimd.memset(minus_half[:], -0.5).then_inc(half_ready, 1)
            pool.wait_ge(half_ready, 1)
            with pool.Fori(0, PAIRS - 1) as p:
                pool.wait_ge(var_ready, p + 1)
                nc.gpsimd.tensor_tensor(rstd[:], var_eps[:], minus_half[:], ALU.pow).then_inc(rstd_ready, 1)
            for r in range(R):
                pool.wait_ge(var_ready, PAIRS + r)
                nc.gpsimd.tensor_tensor(rstd[:, r:r + 1], var_eps[:, r:r + 1], minus_half[:, r:r + 1],
                                        ALU.pow).then_inc(rstd_ready, 1)


def kernel(x, adj, L0_gnn_weight, L0_gnn_wq, L0_gnn_wk):
    import numpy as np
    from concourse import bacc
    from concourse.bass_utils import run_bass_kernel_spmd

    x, adj = np.asarray(x), np.asarray(adj)
    B, N, D = x.shape
    arrays = {
        "x": np.ascontiguousarray(x),
        "x_t": np.ascontiguousarray(
            x.reshape(B // 2, 2, N, D // P, P).transpose(0, 4, 3, 1, 2)).reshape(B // 2, P, -1),
        "adj_t": np.ascontiguousarray(
            adj.reshape(B // 2, 2, N, N // P, P).transpose(0, 4, 1, 3, 2)).reshape(B // 2, P, -1),
        "w": np.ascontiguousarray(L0_gnn_weight),
        "wq_t": np.ascontiguousarray(np.asarray(L0_gnn_wq).T),
        "wk_t": np.ascontiguousarray(np.asarray(L0_gnn_wk).T),
    }
    nc = bacc.Bacc("TRN2", target_bir_lowering=False, num_devices=1)
    args = [nc.dram_tensor(f"in_{name}", a.shape, mybir.dt.from_np(a.dtype), kind="ExternalInput").ap()
            for name, a in arrays.items()]
    out = nc.dram_tensor("out", x.shape, F32, kind="ExternalOutput").ap()
    gnn_resnorm(nc, *args, out)
    r = run_bass_kernel_spmd(nc, [{f"in_{name}": a for name, a in arrays.items()}], core_ids=[0])
    return r.results[0]["out"]
```
